# Optimizing a Trainium2 kernel written in Bass

```python
import numpy as np
import jax
import jax.numpy as jnp

def _softmax(x, axis=-1):
    return jax.nn.softmax(x, axis=axis)

def _gelu(x):
    return jax.nn.gelu(x, approximate=True)

def _silu(x):
    return jax.nn.silu(x)

def _sigmoid(x):
    return jax.nn.sigmoid(x)

def _layernorm(x, axis=-1, eps=1e-05):
    m = jnp.mean(x, axis=axis, keepdims=True)
    v = jnp.var(x, axis=axis, keepdims=True)
    return (x - m) / jnp.sqrt(v + eps)

def _scatter_add(tgt, idx, src, axis=0):
    return tgt.at[idx].add(src)

def _segment_sum(src, seg, n):
    return jax.ops.segment_sum(src, seg, n)
kernel_name = 'mk_dlrm_tower_d1_rec_r8_21fa56'

def setup_inputs(seed: int=0):
    np.random.seed(seed)
    _w = jnp.asarray

    def _rec_inputs():
        import jax
        import jax.numpy as jnp
        _tk = jax.random.key(seed)
        dense_ctx = jax.random.normal(jax.random.fold_in(_tk, 190), (2048, 16), jnp.float32)
        ids = jnp.stack([jax.random.randint(jax.random.fold_in(_tk, 200 + f), (2048,), 0, v, jnp.int32) for f, v in enumerate([12500, 1250, 125000, 1000, 12500, 1000, 12500, 12500, 12500, 12500, 1250, 12500, 1000, 1000, 1000, 125000, 1250, 1250, 12500, 125000, 1000, 1250, 1000, 1250, 1250, 1250, 1000, 1000, 1250, 1000, 1000, 1000])], axis=1)
        tbl_0 = 0.05 * jax.random.normal(jax.random.fold_in(_tk, 500 + 0), (12500, 64), jnp.float32)
        tbl_1 = 0.05 * jax.random.normal(jax.random.fold_in(_tk, 500 + 1), (1250, 64), jnp.float32)
        tbl_2 = 0.05 * jax.random.normal(jax.random.fold_in(_tk, 500 + 2), (125000, 64), jnp.float32)
        tbl_3 = 0.05 * jax.random.normal(jax.random.fold_in(_tk, 500 + 3), (1000, 64), jnp.float32)
        tbl_4 = 0.05 * jax.random.normal(jax.random.fold_in(_tk, 500 + 4), (12500, 64), jnp.float32)
        tbl_5 = 0.05 * jax.random.normal(jax.random.fold_in(_tk, 500 + 5), (1000, 64), jnp.float32)
        tbl_6 = 0.05 * jax.random.normal(jax.random.fold_in(_tk, 500 + 6), (12500, 64), jnp.float32)
        tbl_7 = 0.05 * jax.random.normal(jax.random.fold_in(_tk, 500 + 7), (12500, 64), jnp.float32)
        tbl_8 = 0.05 * jax.random.normal(jax.random.fold_in(_tk, 500 + 8), (12500, 64), jnp.float32)
        tbl_9 = 0.05 * jax.random.normal(jax.random.fold_in(_tk, 500 + 9), (12500, 64), jnp.float32)
        tbl_10 = 0.05 * jax.random.normal(jax.random.fold_in(_tk, 500 + 10), (1250, 64), jnp.float32)
        tbl_11 = 0.05 * jax.random.normal(jax.random.fold_in(_tk, 500 + 11), (12500, 64), jnp.float32)
        tbl_12 = 0.05 * jax.random.normal(jax.random.fold_in(_tk, 500 + 12), (1000, 64), jnp.float32)
        tbl_13 = 0.05 * jax.random.normal(jax.random.fold_in(_tk, 500 + 13), (1000, 64), jnp.float32)
        tbl_14 = 0.05 * jax.random.normal(jax.random.fold_in(_tk, 500 + 14), (1000, 64), jnp.float32)
        tbl_15 = 0.05 * jax.random.normal(jax.random.fold_in(_tk, 500 + 15), (125000, 64), jnp.float32)
        tbl_16 = 0.05 * jax.random.normal(jax.random.fold_in(_tk, 500 + 16), (1250, 64), jnp.float32)
        tbl_17 = 0.05 * jax.random.normal(jax.random.fold_in(_tk, 500 + 17), (1250, 64), jnp.float32)
        tbl_18 = 0.05 * jax.random.normal(jax.random.fold_in(_tk, 500 + 18), (12500, 64), jnp.float32)
        tbl_19 = 0.05 * jax.random.normal(jax.random.fold_in(_tk, 500 + 19), (125000, 64), jnp.float32)
        tbl_20 = 0.05 * jax.random.normal(jax.random.fold_in(_tk, 500 + 20), (1000, 64), jnp.float32)
        tbl_21 = 0.05 * jax.random.normal(jax.random.fold_in(_tk, 500 + 21), (1250, 64), jnp.float32)
        tbl_22 = 0.05 * jax.random.normal(jax.random.fold_in(_tk, 500 + 22), (1000, 64), jnp.float32)
        tbl_23 = 0.05 * jax.random.normal(jax.random.fold_in(_tk, 500 + 23), (1250, 64), jnp.float32)
        tbl_24 = 0.05 * jax.random.normal(jax.random.fold_in(_tk, 500 + 24), (1250, 64), jnp.float32)
        tbl_25 = 0.05 * jax.random.normal(jax.random.fold_in(_tk, 500 + 25), (1250, 64), jnp.float32)
        tbl_26 = 0.05 * jax.random.normal(jax.random.fold_in(_tk, 500 + 26), (1000, 64), jnp.float32)
        tbl_27 = 0.05 * jax.random.normal(jax.random.fold_in(_tk, 500 + 27), (1000, 64), jnp.float32)
        tbl_28 = 0.05 * jax.random.normal(jax.random.fold_in(_tk, 500 + 28), (1250, 64), jnp.float32)
        tbl_29 = 0.05 * jax.random.normal(jax.random.fold_in(_tk, 500 + 29), (1000, 64), jnp.float32)
        tbl_30 = 0.05 * jax.random.normal(jax.random.fold_in(_tk, 500 + 30), (1000, 64), jnp.float32)
        tbl_31 = 0.05 * jax.random.normal(jax.random.fold_in(_tk, 500 + 31), (1000, 64), jnp.float32)
        _rk = jax.random.fold_in(_tk, 7)
        W_top1 = 0.0606339 * jax.random.normal(jax.random.fold_in(_tk, 801), (272, 512), jnp.float32)
        W_top2 = 0.0441942 * jax.random.normal(jax.random.fold_in(_tk, 802), (512, 256), jnp.float32)
        W_top3 = 0.0625 * jax.random.normal(jax.random.fold_in(_tk, 803), (256, 1), jnp.float32)
        b_top1 = jnp.zeros((512,), jnp.float32)
        b_top2 = jnp.zeros((256,), jnp.float32)
        return (dense_ctx, ids, tbl_0, tbl_1, tbl_2, tbl_3, tbl_4, tbl_5, tbl_6, tbl_7, tbl_8, tbl_9, tbl_10, tbl_11, tbl_12, tbl_13, tbl_14, tbl_15, tbl_16, tbl_17, tbl_18, tbl_19, tbl_20, tbl_21, tbl_22, tbl_23, tbl_24, tbl_25, tbl_26, tbl_27, tbl_28, tbl_29, tbl_30, tbl_31, W_top1, b_top1, W_top2, b_top2, W_top3)
    dense_ctx, ids, tbl_0, tbl_1, tbl_2, tbl_3, tbl_4, tbl_5, tbl_6, tbl_7, tbl_8, tbl_9, tbl_10, tbl_11, tbl_12, tbl_13, tbl_14, tbl_15, tbl_16, tbl_17, tbl_18, tbl_19, tbl_20, tbl_21, tbl_22, tbl_23, tbl_24, tbl_25, tbl_26, tbl_27, tbl_28, tbl_29, tbl_30, tbl_31, W_top1, b_top1, W_top2, b_top2, W_top3 = _rec_inputs()

    def _L0_rec_setup():
        import jax, jax.numpy as jnp
        import numpy as np
        EMB_DIM = 64
        NUM_FIELDS = 32
        NUM_PAIRS = NUM_FIELDS * (NUM_FIELDS - 1) // 2
        D1 = 256
        BATCH = 256
        key = jax.random.key(seed)
        k1, k2, k3 = jax.random.split(key, 3)
        feat_emb = jax.random.normal(k1, (BATCH, NUM_FIELDS, EMB_DIM), dtype=jnp.float32)
        lim_k = float(np.sqrt(6.0 / (EMB_DIM + EMB_DIM)))
        kernel = jax.random.uniform(k2, (EMB_DIM, NUM_PAIRS, EMB_DIM), minval=-lim_k, maxval=lim_k, dtype=jnp.float32)
        lim_w = float(np.sqrt(6.0 / (NUM_PAIRS + D1)))
        W = jax.random.uniform(k3, (D1, NUM_PAIRS), minval=-lim_w, maxval=lim_w, dtype=jnp.float32)
        b = jnp.zeros((D1,), dtype=jnp.float32)
        return {'feat_emb': feat_emb, 'kernel': kernel, 'W': W, 'b': b}
    _L0_rec_all = _L0_rec_setup()
    _L0_rec_in = {k: v for k, v in _L0_rec_all.items() if k in ('kernel', 'W', 'b')}
    del _L0_rec_all
    return {'dense_ctx': dense_ctx, 'ids': ids, 'tbl_0': tbl_0, 'tbl_1': tbl_1, 'tbl_2': tbl_2, 'tbl_3': tbl_3, 'tbl_4': tbl_4, 'tbl_5': tbl_5, 'tbl_6': tbl_6, 'tbl_7': tbl_7, 'tbl_8': tbl_8, 'tbl_9': tbl_9, 'tbl_10': tbl_10, 'tbl_11': tbl_11, 'tbl_12': tbl_12, 'tbl_13': tbl_13, 'tbl_14': tbl_14, 'tbl_15': tbl_15, 'tbl_16': tbl_16, 'tbl_17': tbl_17, 'tbl_18': tbl_18, 'tbl_19': tbl_19, 'tbl_20': tbl_20, 'tbl_21': tbl_21, 'tbl_22': tbl_22, 'tbl_23': tbl_23, 'tbl_24': tbl_24, 'tbl_25': tbl_25, 'tbl_26': tbl_26, 'tbl_27': tbl_27, 'tbl_28': tbl_28, 'tbl_29': tbl_29, 'tbl_30': tbl_30, 'tbl_31': tbl_31, 'W_top1': W_top1, 'b_top1': b_top1, 'W_top2': W_top2, 'b_top2': b_top2, 'W_top3': W_top3, 'L0_rec_kernel': _L0_rec_in['kernel'], 'L0_rec_W': _L0_rec_in['W'], 'L0_rec_b': _L0_rec_in['b']}

def reference(dense_ctx, ids, tbl_0, tbl_1, tbl_2, tbl_3, tbl_4, tbl_5, tbl_6, tbl_7, tbl_8, tbl_9, tbl_10, tbl_11, tbl_12, tbl_13, tbl_14, tbl_15, tbl_16, tbl_17, tbl_18, tbl_19, tbl_20, tbl_21, tbl_22, tbl_23, tbl_24, tbl_25, tbl_26, tbl_27, tbl_28, tbl_29, tbl_30, tbl_31, W_top1, b_top1, W_top2, b_top2, W_top3, L0_rec_kernel, L0_rec_W, L0_rec_b):
    import jax
    import jax.numpy as jnp

    def _L0_rec_ref(feat_emb, kernel, W, b):
        import jax, jax.numpy as jnp
        import numpy as np
        EMB_DIM = 64
        NUM_FIELDS = 32
        NUM_PAIRS = NUM_FIELDS * (NUM_FIELDS - 1) // 2
        D1 = 256
        BATCH = 256
        num_fields = feat_emb.shape[1]
        rows, cols = np.triu_indices(num_fields, k=1)
        p = feat_emb[:, rows, :]
        q = feat_emb[:, cols, :]
        pij = jnp.einsum('bpe,dpe,bpd->bp', p, kernel, q)
        return pij @ W.T + b
    e = jnp.stack([tbl_0[ids[:, 0]], tbl_1[ids[:, 1]], tbl_2[ids[:, 2]], tbl_3[ids[:, 3]], tbl_4[ids[:, 4]], tbl_5[ids[:, 5]], tbl_6[ids[:, 6]], tbl_7[ids[:, 7]], tbl_8[ids[:, 8]], tbl_9[ids[:, 9]], tbl_10[ids[:, 10]], tbl_11[ids[:, 11]], tbl_12[ids[:, 12]], tbl_13[ids[:, 13]], tbl_14[ids[:, 14]], tbl_15[ids[:, 15]], tbl_16[ids[:, 16]], tbl_17[ids[:, 17]], tbl_18[ids[:, 18]], tbl_19[ids[:, 19]], tbl_20[ids[:, 20]], tbl_21[ids[:, 21]], tbl_22[ids[:, 22]], tbl_23[ids[:, 23]], tbl_24[ids[:, 24]], tbl_25[ids[:, 25]], tbl_26[ids[:, 26]], tbl_27[ids[:, 27]], tbl_28[ids[:, 28]], tbl_29[ids[:, 29]], tbl_30[ids[:, 30]], tbl_31[ids[:, 31]]], axis=1)
    z = _L0_rec_ref(e, L0_rec_kernel, L0_rec_W, L0_rec_b)
    z = z.reshape(z.shape[0], -1)
    h = jnp.concatenate([z, dense_ctx], axis=1)
    h = jnp.maximum(h @ W_top1 + b_top1, 0.0)
    h = jnp.maximum(h @ W_top2 + b_top2, 0.0)
    y = h @ W_top3
    return y

_drawn_inputs = setup_inputs


def setup_inputs(seed=0):
    import zlib

    import numpy as np

    out = dict(_drawn_inputs(seed))
    spreads = {'b_top1': (0.0, 0.1), 'b_top2': (0.0, 0.1), 'L0_rec_b': (0.0, 0.1)}
    factors = {'tbl_0': 3.205,
     'tbl_1': 3.03,
     'tbl_2': 3.142,
     'tbl_3': 3.196,
     'tbl_4': 3.498,
     'tbl_5': 3.274,
     'tbl_6': 2.996,
     'tbl_7': 3.006,
     'tbl_8': 3.309,
     'tbl_9': 3.026,
     'tbl_10': 3.296,
     'tbl_11': 3.068,
     'tbl_12': 3.299,
     'tbl_13': 3.289,
     'tbl_14': 2.987,
     'tbl_15': 3.221,
     'tbl_16': 3.411,
     'tbl_17': 3.241,
     'tbl_18': 3.428,
     'tbl_19': 3.013,
     'tbl_20': 3.087,
     'tbl_21': 3.378,
     'tbl_22': 3.503,
     'tbl_23': 2.86,
     'tbl_24': 3.308,
     'tbl_25': 2.942,
     'tbl_26': 3.183,
     'tbl_27': 3.213,
     'tbl_28': 3.387,
     'tbl_29': 3.2,
     'tbl_30': 3.195,
     'tbl_31': 3.213}
    for name, (base, spread) in spreads.items():
        noise = np.random.default_rng([zlib.crc32(name.encode()), seed]).standard_normal(out[name].shape)
        drawn = base * np.exp(spread * noise) if base else spread * noise
        out[name] = jnp.asarray(drawn.astype(out[name].dtype))
    for name, factor in factors.items():
        out[name] = (out[name] * factor).astype(out[name].dtype)
    return out
```

```python
from contextlib import ExitStack

import numpy as np

import concourse.bass as bass
from concourse import mybir

F32, F32R, I32 = mybir.dt.float32, mybir.dt.float32r, mybir.dt.int32
ALU = mybir.AluOpType
ACT = mybir.ActivationFunctionType

BATCH, FIELDS, EMB, DENSE = 2048, 32, 64, 16
D1, H1, H2 = 256, 512, 256
P = 128

HALVES = 2
HB = BATCH // HALVES
BT = HB // P
CHUNK = 512
CHUNKS = HB // CHUNK
BLOCKS = FIELDS // 2

TILES = [(c, m, jj) for c in range(BLOCKS) for m in range(c + 1) for jj in ((0, 1) if m < c else (1,))]
NT = len(TILES)
START = [TILES.index((c, 0, 0 if c else 1)) for c in range(BLOCKS)]
GROUP = 4
SLOTS = 16
KT_TILES = GROUP * SLOTS
KT = NT // KT_TILES
PIECE = 8
PIECES = NT // PIECE

NE, NP, NTB, NM, NK = 4, 8, 2, 2, 2


def pij_row(t, parity):
    return t // KT_TILES, 32 * (t % GROUP) + 2 * (t // GROUP % SLOTS) + parity


DENSE_ROWS = [pij_row(START[c] + 2 * c, 1) for c in range(BLOCKS)]


def transpose_at(c):
    if c == 0:
        return 0
    return START[c - 1] if c < 6 else START[c] - 8


def dlrm_program(nc, ids, tables, kern, w_ext, dense_t, w1, b1, w2, b2, w3, b0, out):
    ctx = ExitStack()
    with ctx:
        def sb(name, shape, dt=F32):
            return ctx.enter_context(nc.sbuf_tensor(name, shape, dt))

        def sem(name):
            return ctx.enter_context(nc.semaphore(name))

        ids_sb = sb("ids_sb", [P, HALVES * BT * FIELDS], I32)
        ident = sb("ident", [P, P])
        selector = sb("selector", [P, 62])
        gathered = sb("gathered", [P, NE, BT, 2 * EMB])
        emb_t = sb("emb_t", [P, BLOCKS, HB])
        q_twice = sb("q_twice", [P, 2, HB])
        q_split = sb("q_split", [P, NM, 2, HB], F32R)
        k_raw = sb("k_raw", [P, NK, PIECE * P])
        k_hi = sb("k_hi", [P, NK, PIECE * P], F32R)
        k_lo = sb("k_lo", [P, NK, PIECE * P], F32R)
        prod = sb("prod", [P, NP, HB])
        pij = sb("pij", [P, KT, HB])
        w_fold = sb("w_fold", [P, KT, H1])
        w2_sb = sb("w2_sb", [P, H1 // P, H2])
        w3_sb = sb("w3_sb", [P, H2 // P])
        b0_sb = sb("b0_sb", [P, D1 // P])
        b1_sb = sb("b1_sb", [P, H1 // P])
        b1_fold = sb("b1_fold", [P, H1 // P])
        b2_sb = sb("b2_sb", [P, H2 // P])
        y_sb = sb("y_sb", [1, HB])
        w_ext_sb = prod[:, 0:3, 0:KT * P]
        w1_sb = prod[:, 3:6, 0:H1]
        h1_sb = prod[:, 0:H1 // P, :]
        h2_sb = prod[:, H1 // P:H1 // P + H2 // P, :]

        t_ps = ctx.enter_context(nc.psum_tensor("t_ps", [P, NTB, HB], F32))
        acc_ps = ctx.enter_context(nc.psum_tensor("acc_ps", [P, HB], F32))
        tr_ps = ctx.enter_context(nc.psum_tensor("tr_ps", [P, HB], F32))
        bank = [t_ps[:, n // CHUNKS, n % CHUNKS * CHUNK:(n % CHUNKS + 1) * CHUNK] for n in range(NTB * CHUNKS)]

        ids_in = sem("ids_in")
        zeroed = sem("zeroed")
        ident_ready = sem("ident_ready")
        selector_ready = sem("selector_ready")
        fold_in = sem("fold_in")
        weights_in = sem("weights_in")
        fold_ps = sem("fold_ps")
        w_folded = sem("w_folded")
        b_folded = sem("b_folded")
        gather_in = [sem(f"gather_in{n}") for n in range(NE)]
        transposed = sem("transposed")
        emb_ready = sem("emb_ready")
        twice_in = sem("twice_in")
        q_hi_ready = sem("q_hi_ready")
        q_lo_ready = sem("q_lo_ready")
        k_in = [sem(f"k_in{n}") for n in range(NK)]
        k_hi_ready = sem("k_hi_ready")
        k_lo_ready = sem("k_lo_ready")
        t_ready = sem("t_ready")
        prod_ready = sem("prod_ready")
        summed = sem("summed")
        pij_ready = sem("pij_ready")
        dense_in = sem("dense_in")
        h1_ps = sem("h1_ps")
        h1_ready = sem("h1_ready")
        h2_ps = sem("h2_ps")
        h2_ready = sem("h2_ready")
        y_ps = sem("y_ps")
        y_ready = sem("y_ready")
        out_done = sem("out_done")
        y_free = sem("y_free")

        M1, M2 = H1 // P, H2 // P

        def at(h, per_half, n):
            return h * per_half + max(n, 0) + 1

        def start_at_one(engine, semaphores):
            for semaphore in semaphores:
                engine.sem_inc(semaphore, 1)

        block = ctx.enter_context(nc.Block())

        @block.gpsimd
        def _(pool):
            nc.gpsimd.memset(ident[:], 0.0).then_inc(zeroed, 1)
            pool.wait_ge(zeroed, 1)
            nc.gpsimd.affine_select(out=ident[:], in_=ident[:], compare_op=ALU.not_equal, fill=1.0, base=0,
                                    pattern=[[-1, P]], channel_multiplier=1).then_inc(ident_ready, 1)
            pool.wait_ge(ids_in, 16)
            for n in range(HALVES * BLOCKS):
                h, c = divmod(n, BLOCKS)
                if n >= NE:
                    pool.wait_ge(transposed, at(0, BLOCKS, n - NE + 1))
                for f in (2 * c, 2 * c + 1):
                    for bt in range(BT):
                        col = (h * BT + bt) * FIELDS + f
                        nc.gpsimd.indirect_dma_start(
                            out=gathered[:, c % NE, bt, f % 2 * EMB:(f % 2 + 1) * EMB], out_offset=None, in_=tables[f],
                            in_offset=bass.IndirectOffsetOnAxis(ap=ids_sb[:, col:col + 1], axis=0),
                        ).then_inc(gather_in[c % NE], 16)

        @block.sync
        def _(sp):
            start_at_one(sp, [y_free])
            sp.dma_start(ids_sb[:].rearrange("p (t f) -> p t f", f=FIELDS),
                         ids.rearrange("(t p) f -> p t f", p=P)).then_inc(ids_in, 16)

            def load_piece(h, k):
                sp.wait_ge(k_lo_ready, at(h, PIECES, k - NK + 1))
                for half in range(2):
                    sp.dma_start(k_raw[64 * half:64 * half + 64, k % NK, :],
                                 kern[:, k * PIECE * P:(k + 1) * PIECE * P]).then_inc(k_in[k % NK], 16)

            def double(h, c):
                sp.wait_ge(emb_ready, at(h, BLOCKS, c + 1))
                for jj in range(2):
                    for half in range(2):
                        sp.dma_start(q_twice[64 * half:64 * half + 64, jj, :],
                                     emb_t[EMB * jj:EMB * jj + EMB, c, :]).then_inc(twice_in, 16)

            def load_dense(h, kt):
                sp.wait_ge(pij_ready, at(h, KT, kt + 1))
                for n, (at_kt, row) in enumerate(DENSE_ROWS):
                    if at_kt == kt:
                        sp.dma_start(pij[row:row + 1, kt, :], dense_t[n:n + 1, bass.ds(column[0], HB)]).then_inc(dense_in, 16)

            steps = [(PIECE * (k - 2) + 2, load_piece, k) for k in range(PIECES)]
            steps += [(transpose_at(c) + 1, double, c) for c in range(BLOCKS)]
            steps += [(KT_TILES * (kt + 1) + 8, load_dense, kt) for kt in range(KT)]
            steps.sort(key=lambda s: s[0])
            column = []
            with sp.Fori(0, HALVES) as h:
                column[:] = [sp.snap(h * HB)]
                for _, step, n in steps:
                    step(h, n)
                sp.wait_ge(y_ready, at(h, CHUNKS, CHUNKS))
                sp.dma_start(out[:, bass.ds(column[0], HB)], y_sb[:]).then_inc(out_done, 16)
                sp.wait_ge(out_done, (h + 1) * 16)
                sp.sem_inc(y_free, 1)
            sp.wait_ge(out_done, 16 * HALVES)

        @block.scalar
        def _(act):
            start_at_one(act, [k_hi_ready, emb_ready, q_hi_ready, pij_ready, h1_ready, h2_ready, y_ready])
            for k in range(2):
                act.dma_start(w_ext_sb[:, k, :], w_ext[k * P:(k + 1) * P, :]).then_inc(fold_in, 16)
                act.dma_start(w1_sb[:, k, :], w1[k * P:(k + 1) * P, :]).then_inc(fold_in, 16)
            act.dma_start(w_ext_sb[0:DENSE, 2, :], w_ext[D1:D1 + DENSE, :]).then_inc(fold_in, 16)
            act.dma_start(w1_sb[0:DENSE, 2, :], w1[D1:D1 + DENSE, :]).then_inc(fold_in, 16)
            act.dma_start(b0_sb[:], b0).then_inc(fold_in, 16)
            act.dma_start(b1_sb[:], b1).then_inc(weights_in, 16)
            act.dma_start(b2_sb[:], b2).then_inc(weights_in, 16)
            act.dma_start(w2_sb[:], w2.rearrange("(k p) n -> p k n", p=P)).then_inc(weights_in, 16)
            act.dma_start(w3_sb[:], w3).then_inc(weights_in, 16)

            def copy_fold():
                act.wait_ge(fold_ps, 1)
                nc.scalar.copy(w_fold[:], t_ps[:].rearrange("p a (b n) -> p (a b) n", n=H1)).then_inc(w_folded, 1)

            def split_piece(h, k):
                act.wait_ge(k_in[k % NK], (h * (PIECES // NK) + k // NK + 1) * 32)
                act.wait_ge(t_ready, at(h, NT, (k - NK + 1) * PIECE))
                nc.scalar.copy(k_hi[:, k % NK, :], k_raw[:, k % NK, :]).then_inc(k_hi_ready, 1)

            def copy_block(h, c):
                act.wait_ge(transposed, at(h, BLOCKS, c + 1))
                act.wait_ge(prod_ready, at(h, NT, 0))
                act.wait_ge(q_lo_ready, at(h, FIELDS, 2 * c))
                nc.scalar.copy(emb_t[:, c, :], tr_ps[:]).then_inc(emb_ready, 1)

            def split_block(h, c):
                act.wait_ge(twice_in, (h * BLOCKS + c + 1) * 64)
                act.wait_ge(t_ready, at(h, NT, START[c - NM + 1] if c >= NM else 0))
                for jj in range(2):
                    nc.scalar.copy(q_split[:, c % NM, jj, :], q_twice[:, jj, :]).then_inc(q_hi_ready, 1)

            def copy_pij(h, kt):
                act.wait_ge(summed, at(h, NT // GROUP, (kt + 1) * SLOTS))
                nc.scalar.copy(pij[:, kt, :], acc_ps[:]).then_inc(pij_ready, 1)

            steps = [(PIECE * (k - 1) + 1, 0, split_piece, k) for k in range(PIECES)]
            steps += [(transpose_at(c), 2 * c + 1, copy_block, c) for c in range(BLOCKS)]
            steps += [(min(transpose_at(c) + 4, START[c]), 2 * c + 2, split_block, c) for c in range(BLOCKS)]
            steps += [(KT_TILES * (kt + 1) + 5, 0, copy_pij, kt) for kt in range(KT)]
            steps.sort(key=lambda s: s[:2])
            copy_fold()
            act.wait_ge(weights_in, 64)
            act.wait_ge(b_folded, 1)
            with act.Fori(0, HALVES) as h:
                for _, _, step, n in steps:
                    step(h, n)
                for n in range(CHUNKS):
                    for m in range(M1):
                        act.wait_ge(h1_ps, at(h, M1 * CHUNKS, M1 * n + m + 1))
                        nc.scalar.activation(h1_sb[:, m, n * CHUNK:(n + 1) * CHUNK], bank[m], ACT.Relu,
                                             bias=b1_fold[:, m:m + 1]).then_inc(h1_ready, 1)
                for n in range(CHUNKS):
                    for m in range(M2):
                        act.wait_ge(h2_ps, at(h, M2 * CHUNKS, M2 * n + m + 1))
                        nc.scalar.activation(h2_sb[:, m, n * CHUNK:(n + 1) * CHUNK], tr_ps[:, m * CHUNK:(m + 1) * CHUNK],
                                             ACT.Relu, bias=b2_sb[:, m:m + 1]).then_inc(h2_ready, 1)
                act.wait_ge(y_free, at(h, 1, 0))
                for n in range(CHUNKS):
                    act.wait_ge(y_ps, at(h, CHUNKS, n + 1))
                    nc.scalar.copy(y_sb[:, n * CHUNK:(n + 1) * CHUNK], acc_ps[0:1, n * CHUNK:(n + 1) * CHUNK]).then_inc(y_ready, 1)

        @block.vector
        def _(dve):
            start_at_one(dve, [k_lo_ready, q_lo_ready, prod_ready])
            nc.vector.memset(selector[:], 0.0).then_inc(selector_ready, 1)
            dve.wait_ge(selector_ready, 1)
            nc.vector.memset(selector[0:EMB, 30:31], 1.0).then_inc(selector_ready, 1)
            nc.vector.memset(selector[EMB:P, 31:32], 1.0).then_inc(selector_ready, 1)
            dve.wait_ge(fold_ps, 1)
            dve.wait_ge(weights_in, 64)
            nc.vector.tensor_tensor(b1_fold[:], tr_ps[:, 0:M1], b1_sb[:], ALU.add).then_inc(b_folded, 1)

            def split_piece(h, k):
                dve.wait_ge(k_hi_ready, at(h, PIECES, k + 1))
                dve.wait_ge(t_ready, at(h, NT, (k - NK + 1) * PIECE))
                nc.vector.tensor_tensor(k_lo[:, k % NK, :], k_raw[:, k % NK, :], k_hi[:, k % NK, :].bitcast(F32),
                                        ALU.subtract).then_inc(k_lo_ready, 1)

            def split_block(h, c):
                for jj in range(2):
                    dve.wait_ge(q_hi_ready, at(h, FIELDS, 2 * c + jj + 1))
                    q = q_split[EMB:P, c % NM, jj, :]
                    nc.vector.tensor_tensor(q, q_twice[EMB:P, jj, :], q.bitcast(F32), ALU.subtract).then_inc(q_lo_ready, 1)

            def multiply(h, t):
                c, m, jj = TILES[t]
                if t == 0:
                    dve.wait_ge(w_folded, 1)
                    dve.wait_ge(y_ps, at(h, CHUNKS, 0))
                dve.wait_ge(t_ready, at(h, NT, t + 1))
                dve.wait_ge(emb_ready, at(h, BLOCKS, m + 1))
                dve.wait_ge(summed, at(h, NT // GROUP, (t - NP) // GROUP + 1))
                nc.vector.tensor_tensor(prod[:, t % NP, :], t_ps[:, t % NTB, :], emb_t[:, m, :],
                                        ALU.mult).then_inc(prod_ready, 1)

            steps = [(PIECE * (k - 1) + 2, 0, split_piece, k) for k in range(PIECES)]
            steps += [(min(transpose_at(c) + 5, START[c]), 1, split_block, c) for c in range(BLOCKS)]
            steps += [(t, 2, multiply, t) for t in range(NT)]
            steps.sort(key=lambda s: s[:2])
            with dve.Fori(0, HALVES) as h:
                for _, _, step, n in steps:
                    step(h, n)

        @block.tensor
        def _(pe):
            start_at_one(pe, [t_ready, transposed, summed, h1_ps, h2_ps, y_ps])
            pe.wait_ge(fold_in, 7 * 16)
            for kt in range(KT):
                for k in range(3):
                    rows = P if k < 2 else DENSE
                    nc.tensor.matmul(bank[kt], w_ext_sb[0:rows, k, kt * P:(kt + 1) * P], w1_sb[0:rows, k, :],
                                     start=k == 0, stop=k == 2)
            for m in range(M1):
                for k in range(2):
                    last = nc.tensor.matmul(tr_ps[:, m:m + 1], w1_sb[:, k, m * P:(m + 1) * P], b0_sb[:, k:k + 1],
                                            start=k == 0, stop=k == 1)
            last.then_inc(fold_ps, 1)
            pe.wait_ge(w_folded, 1)
            pe.wait_ge(b_folded, 1)
            pe.wait_ge(ident_ready, 1)
            pe.wait_ge(selector_ready, 3)

            def transpose_block(h, c):
                pe.wait_ge(gather_in[c % NE], (h * (BLOCKS // NE) + c // NE + 1) * (2 * BT * 16))
                if c == 0:
                    pe.wait_ge(h2_ready, at(h, M2 * CHUNKS, 0))
                else:
                    pe.wait_ge(emb_ready, at(h, BLOCKS, c))
                for bt in range(BT):
                    last = nc.tensor.transpose(tr_ps[:, bt * P:(bt + 1) * P], gathered[:, c % NE, bt, :], ident[:])
                last.then_inc(transposed, 1)

            def interact(h, t):
                c, m, jj = TILES[t]
                k, slot = t // PIECE, t % PIECE
                if slot == 0:
                    pe.wait_ge(k_hi_ready, at(h, PIECES, k + 1))
                    pe.wait_ge(k_lo_ready, at(h, PIECES, k + 1))
                if t == START[c]:
                    pe.wait_ge(q_lo_ready, at(h, FIELDS, 2 * c + 2))
                if t == 0:
                    pe.wait_ge(h1_ready, at(h, M1 * CHUNKS, 0))
                pe.wait_ge(prod_ready, at(h, NT, t - NTB + 1))
                for n in range(CHUNKS):
                    cols = slice(n * CHUNK, (n + 1) * CHUNK)
                    for part, kk in enumerate((k_hi, k_lo)):
                        last = nc.tensor.matmul(t_ps[:, t % NTB, cols], kk[:, k % NK, slot * P:(slot + 1) * P],
                                                q_split[:, c % NM, jj, cols], start=part == 0, stop=part == 1)
                last.then_inc(t_ready, 1)

            def sum_group(h, g):
                s = g % SLOTS
                if s == 0:
                    pe.wait_ge(y_ready, at(h, CHUNKS, 0))
                    pe.wait_ge(pij_ready, at(h, KT, g // SLOTS))
                pe.wait_ge(prod_ready, at(h, NT, GROUP * (g + 1)))
                for n in range(CHUNKS):
                    cols = slice(n * CHUNK, (n + 1) * CHUNK)
                    for q in range(GROUP):
                        last = nc.tensor.matmul(acc_ps[32 * q:32 * q + 32, cols], selector[:, 30 - 2 * s:62 - 2 * s],
                                                prod[:, (GROUP * g + q) % NP, cols], start=s == 0, stop=s == SLOTS - 1)
                last.then_inc(summed, 1)

            steps = [(transpose_at(c), 0, transpose_block, c) for c in range(BLOCKS)]
            steps += [(t, 1, interact, t) for t in range(NT)]
            steps += [(GROUP * (g + 2) - 1, 2, sum_group, g) for g in range(NT // GROUP)]
            steps.sort(key=lambda s: s[:2])
            with pe.Fori(0, HALVES) as h:
                for _, _, step, n in steps:
                    step(h, n)
                pe.wait_ge(pij_ready, at(h, KT, KT))
                pe.wait_ge(dense_in, (h + 1) * len(DENSE_ROWS) * 16)
                pe.wait_ge(prod_ready, at(h, NT, NT))
                pe.wait_ge(emb_ready, at(h, BLOCKS, BLOCKS))
                for n in range(CHUNKS):
                    for m in range(M1):
                        if n:
                            pe.wait_ge(h1_ready, at(h, M1 * CHUNKS, M1 * (n - 1) + m + 1))
                        for kt in range(KT):
                            last = nc.tensor.matmul(bank[m], w_fold[:, kt, m * P:(m + 1) * P],
                                                    pij[:, kt, n * CHUNK:(n + 1) * CHUNK], start=kt == 0, stop=kt == KT - 1)
                        last.then_inc(h1_ps, 1)
                for n in range(CHUNKS):
                    pe.wait_ge(h1_ready, at(h, M1 * CHUNKS, M1 * (n + 1)))
                    for m in range(M2):
                        if n:
                            pe.wait_ge(h2_ready, at(h, M2 * CHUNKS, M2 * (n - 1) + m + 1))
                        for k in range(M1):
                            last = nc.tensor.matmul(tr_ps[:, m * CHUNK:(m + 1) * CHUNK], w2_sb[:, k, m * P:(m + 1) * P],
                                                    h1_sb[:, k, n * CHUNK:(n + 1) * CHUNK], start=k == 0, stop=k == M1 - 1)
                        last.then_inc(h2_ps, 1)
                for n in range(CHUNKS):
                    pe.wait_ge(h2_ready, at(h, M2 * CHUNKS, M2 * (n + 1)))
                    for k in range(M2):
                        last = nc.tensor.matmul(acc_ps[0:1, n * CHUNK:(n + 1) * CHUNK], w3_sb[:, k:k + 1],
                                                h2_sb[:, k, n * CHUNK:(n + 1) * CHUNK], start=k == 0, stop=k == M2 - 1)
                    last.then_inc(y_ps, 1)


def tile_layout(L0_rec_kernel, L0_rec_W):
    pair = {}
    for i in range(FIELDS):
        for j in range(i + 1, FIELDS):
            pair[i, j] = len(pair)
    kern = np.zeros((EMB, NT, 2, EMB), L0_rec_kernel.dtype)
    w_ext = np.zeros((D1 + DENSE, KT, P), L0_rec_W.dtype)
    for t, (c, m, jj) in enumerate(TILES):
        for parity in range(2):
            i, j = 2 * m + parity, 2 * c + jj
            if i < j:
                kern[:, t, parity, :] = L0_rec_kernel[:, pair[i, j], :]
                kt, row = pij_row(t, parity)
                w_ext[0:D1, kt, row] = L0_rec_W[:, pair[i, j]]
    for n, (kt, row) in enumerate(DENSE_ROWS):
        w_ext[D1 + n, kt, row] = 1
    return kern.reshape(EMB, NT * P), w_ext.reshape(D1 + DENSE, KT * P)


def kernel(**inputs):
    import concourse.bacc as bacc
    from concourse.bass_utils import run_bass_kernel_spmd

    nc = bacc.Bacc("TRN2", target_bir_lowering=False, num_devices=1)
    arrays = {}

    def given(name, a):
        a = np.ascontiguousarray(a)
        arrays[name] = a
        return nc.dram_tensor(name, a.shape, mybir.dt.from_np(a.dtype), kind="ExternalInput").ap()

    def by_partition(v):
        return np.asarray(v).reshape(-1, P).T

    kern, w_ext = tile_layout(np.asarray(inputs["L0_rec_kernel"]), np.asarray(inputs["L0_rec_W"]))
    tables = [given(f"tbl_{f}", np.asarray(inputs[f"tbl_{f}"])) for f in range(FIELDS)]
    out = nc.dram_tensor("y", (1, BATCH), F32, kind="ExternalOutput").ap()
    dlrm_program(
        nc, given("ids", np.asarray(inputs["ids"])), tables, given("kern", kern), given("w_ext", w_ext),
        given("dense_t", np.asarray(inputs["dense_ctx"]).T), given("w1", np.asarray(inputs["W_top1"])),
        given("b1", by_partition(inputs["b_top1"])), given("w2", np.asarray(inputs["W_top2"])),
        given("b2", by_partition(inputs["b_top2"])), given("w3", by_partition(inputs["W_top3"])),
        given("b0", by_partition(inputs["L0_rec_b"])), out)
    r = run_bass_kernel_spmd(nc, [arrays], core_ids=[0])
    return r.results[0]["y"].reshape(BATCH, 1)
```

```python
from contextlib import ExitStack

import numpy as np

import concourse.bass as bass
from concourse import mybir

F32, F32R, I32 = mybir.dt.float32, mybir.dt.float32r, mybir.dt.int32
ALU = mybir.AluOpType
ACT = mybir.ActivationFunctionType

BATCH, FIELDS, EMB, DENSE = 2048, 32, 64, 16
D1, H1, H2 = 256, 512, 256
P = 128

PB = 512
PARTS = BATCH // PB
BT = PB // P
BLOCKS = FIELDS // 2
M1, M2 = H1 // P, H2 // P

UNITS = []
for _c in range(BLOCKS):
    UNITS += [((_c, m, 0), (_c, m, 1)) for m in range(_c)]
    if _c % 2 == 0:
        UNITS.append(((_c, _c, 1), (_c + 1, _c + 1, 1)))
TILES = [tile for unit in UNITS for tile in unit]
NU, NT = len(UNITS), len(TILES)
FIRST_USE = [min(u for u in range(NU) if any(tile[0] == c for tile in UNITS[u])) for c in range(BLOCKS)]
LAST_Q_USE = [max(u for u in range(NU) if any(tile[0] == c for tile in UNITS[u])) for c in range(BLOCKS)]
LAST_USE = [max(u for u in range(NU) if any(tile[1] == c for tile in UNITS[u])) for c in range(BLOCKS)]

COLS = 4
SLOTS = 16
KT_TILES = COLS * SLOTS
KT = NT // KT_TILES
SUM_UNITS = 4
NS = NU // SUM_UNITS
SUMS_PER_KT = NS // KT
PIECE = 4
PIECES = NU // PIECE
KEPT = 4
STREAMED = PIECES - KEPT
VECTOR_PIECES_FIRST, VECTOR_PIECES = 20, 14

NE, NP, NTB, NM, NR, NK, NA = 8, 8, 3, 2, 2, 4, 2


def pij_row(t, parity):
    return t // KT_TILES, 32 * (t % COLS) + 2 * (t // COLS % SLOTS) + parity


DENSE_ROWS = [pij_row(TILES.index((c, c, 1)), 1) for c in range(BLOCKS)]

LEAD = 5
TRANSPOSE_AT = [max(FIRST_USE[c] - LEAD, FIRST_USE[c - 1]) if c else 0 for c in range(BLOCKS)]

TRANSPOSE, LAYER1, LAYER2, LAYER3, PRODUCT, SUMS = range(6)
LAYER1_AT, LAYER2_AT, LAYER3_AT = (0, 0, 2, 5), (9, 12), (15,)
ORDER = [(TRANSPOSE_AT[c], TRANSPOSE, c) for c in range(BLOCKS)]
ORDER += [(u, LAYER1, m) for m, u in enumerate(LAYER1_AT)]
ORDER += [(u, LAYER2, m) for m, u in enumerate(LAYER2_AT)]
ORDER += [(u, LAYER3, 0) for u in LAYER3_AT]
ORDER += [(u, PRODUCT, u) for u in range(NU)]
ORDER += [(SUM_UNITS * (s + 2) - 1, SUMS, s) for s in range(NS)]
ORDER.sort(key=lambda s: s[:2])
MLP = (LAYER1, LAYER2, LAYER3)
T_USERS = [(what, n) for _, what, n in ORDER if what != SUMS]
T_BUFFER = {user: at % NTB for at, user in enumerate(T_USERS)}


def before_in_buffer(user, part):
    first, last = (isinstance(part, int) and part == n for n in (0, PARTS))
    users = [x for x in T_USERS if T_BUFFER[x] == T_BUFFER[user]]
    earlier = [x for x in users[:users.index(user)] if not (first and x[0] in MLP or last and x[0] not in MLP)]
    if earlier:
        return earlier[-1], False
    return (None, False) if first or last else (users[-1], True)


def dlrm_program(nc, ids, tables, kern, w_ext, dense_t, w1, b1, w2, b2, w3, b0, out):
    ctx = ExitStack()
    with ctx:
        def sb(name, shape, dt=F32):
            return ctx.enter_context(nc.sbuf_tensor(name, shape, dt))

        def sem(name):
            return ctx.enter_context(nc.semaphore(name))

        ids_sb = sb("ids_sb", [P, PARTS * BT * FIELDS], I32)
        ident = sb("ident", [P, P])
        selector = sb("selector", [P, 62])
        gathered = sb("gathered", [P, NE, BT, 2 * EMB])
        emb_t = sb("emb_t", [P, BLOCKS, PB])
        q_split = sb("q_split", [P, NM, 2, PB], F32R)
        k_raw = sb("k_raw", [P, NR, PIECE * 2 * P])
        k_hi = sb("k_hi", [P, KEPT + NK, PIECE * 2 * P], F32R)
        k_lo = sb("k_lo", [P, KEPT + NK, PIECE * 2 * P], F32R)
        prod = sb("prod", [P, NP, 2, PB])
        pij = sb("pij", [P, KT, PB])
        h1_sb = sb("h1_sb", [P, M1, PB])
        h2_sb = sb("h2_sb", [P, M2, PB])
        y_sb = sb("y_sb", [1, PB])
        w_fold = sb("w_fold", [P, KT, H1])
        w2_sb = sb("w2_sb", [P, M1, H2])
        w3_sb = sb("w3_sb", [P, M2])
        b0_sb = sb("b0_sb", [P, D1 // P])
        b1_sb = sb("b1_sb", [P, M1])
        b1_fold = sb("b1_fold", [P, M1])
        b2_sb = sb("b2_sb", [P, M2])
        w_ext_sb = prod[:, 0:3, 0, :]
        w1_sb = prod[:, 0:3, 1, :]
        kept_raw = prod[:, NP - KEPT:NP].rearrange("p k a n -> p k (a n)")

        t_ps = ctx.enter_context(nc.psum_tensor("t_ps", [P, NTB, 2, PB], F32))
        acc_ps = ctx.enter_context(nc.psum_tensor("acc_ps", [P, NA, PB], F32))

        def t_buffer(what, n):
            buffer = t_ps[:, T_BUFFER[what, n]]
            return buffer if what == PRODUCT else buffer[:, 0]

        ids_in = sem("ids_in")
        zeroed = sem("zeroed")
        ident_ready = sem("ident_ready")
        selector_ready = sem("selector_ready")
        fold_in = sem("fold_in")
        weights_in = sem("weights_in")
        fold_ps = sem("fold_ps")
        w_folded = sem("w_folded")
        b_folded = sem("b_folded")
        gather_in = [sem(f"gather_in{n}") for n in range(NE)]
        transposed = sem("transposed")
        emb_ready = sem("emb_ready")
        q_hi_ready = sem("q_hi_ready")
        q_lo_ready = sem("q_lo_ready")
        kept_in = sem("kept_in")
        kept_hi_ready = sem("kept_hi_ready")
        kept_lo_ready = sem("kept_lo_ready")
        k_in = [sem(f"k_in{n}") for n in range(NR)]
        k_hi_ready = sem("k_hi_ready")
        k_lo_vector = sem("k_lo_vector")
        k_lo_pool = sem("k_lo_pool")
        t_ready = sem("t_ready")
        prod_ready = sem("prod_ready")
        summed = sem("summed")
        pij_ready = sem("pij_ready")
        dense_in = [sem(f"dense_in{kt}") for kt in range(KT)]
        h1_ps = sem("h1_ps")
        h1_ready = sem("h1_ready")
        h2_ps = sem("h2_ps")
        h2_ready = sem("h2_ready")
        y_ps = sem("y_ps")
        y_ready = sem("y_ready")
        out_done = sem("out_done")

        def wait(engine, semaphore, part, per_part, n):
            if isinstance(part, int) and part * per_part + n <= 0:
                return
            engine.wait_ge(semaphore, part * per_part + n)

        def vector_pieces(part):
            return VECTOR_PIECES_FIRST if isinstance(part, int) and part == 0 else VECTOR_PIECES

        def wait_for_k_lo(engine, part, n):
            first = isinstance(part, int) and part == 0
            by_vector = 0 <= n < vector_pieces(part)
            semaphore, in_first, in_other, at = (
                (k_lo_vector, VECTOR_PIECES_FIRST, VECTOR_PIECES, n + 1) if by_vector else
                (k_lo_pool, STREAMED - VECTOR_PIECES_FIRST, STREAMED - VECTOR_PIECES, n - vector_pieces(part) + 1 if n >= 0 else n + 1))
            wait(engine, semaphore, part, in_other, at if first else at + in_first - in_other)

        def wait_for_k_buffer(engine, part, n):
            before = n - NK + KEPT + 1 if n >= NK else n - NK + 1
            wait(engine, t_ready, part, NU, before * PIECE)

        def split_piece_lo(engine, part, n):
            wait(engine, k_hi_ready, part, STREAMED, n + 1)
            wait_for_k_buffer(engine, part, n)
            at = KEPT + n % NK
            engine.tensor_tensor(k_lo[:, at, :], k_raw[:, n % NR, :], k_hi[:, at, :].bitcast(F32),
                                 ALU.subtract).then_inc(k_lo_vector if n < vector_pieces(part) else k_lo_pool, 1)

        def over_parts(engine, part_steps, mlp_steps):
            part_steps(0)
            with engine.Fori(1, PARTS) as part:
                part_steps(part)
            mlp_steps(PARTS - 1)

        block = ctx.enter_context(nc.Block())

        @block.gpsimd
        def _(pool):
            nc.gpsimd.memset(ident[:], 0.0).then_inc(zeroed, 1)
            pool.wait_ge(zeroed, 1)
            nc.gpsimd.affine_select(out=ident[:], in_=ident[:], compare_op=ALU.not_equal, fill=1.0, base=0,
                                    pattern=[[-1, P]], channel_multiplier=1).then_inc(ident_ready, 1)
            pool.wait_ge(ids_in, 16)
            def gather_field(part, f):
                c, jj = divmod(f, 2)
                if jj == 0:
                    wait(pool, transposed, part, BLOCKS, c - NE + 1)
                for bt in range(BT):
                    col = (part * BT + bt) * FIELDS + f
                    nc.gpsimd.indirect_dma_start(
                        out=gathered[:, c % NE, bt, jj * EMB:(jj + 1) * EMB], out_offset=None, in_=tables[f],
                        in_offset=bass.IndirectOffsetOnAxis(ap=ids_sb[:, col:col + 1], axis=0),
                    ).then_inc(gather_in[c % NE], 16)

            def split_piece(part, n):
                split_piece_lo(pool, part, n)

            steps = [(NU * part + (TRANSPOSE_AT[c - NE] if c >= NE else TRANSPOSE_AT[c + NE] - NU) + 2 * (f % 2), gather_field, part, f)
                     for part in range(PARTS) for f in range(FIELDS) for c in (f // 2,)]
            steps += [(NU * part + PIECE * (KEPT + n - 3) + 2, split_piece, part, n)
                      for part in range(PARTS) for n in range(vector_pieces(part), STREAMED)]
            for _, step, part, n in sorted(steps, key=lambda s: s[0]):
                step(part, n)

        @block.sync
        def _(sp):
            sp.dma_start(ids_sb[:].rearrange("p (t f) -> p t f", f=FIELDS),
                         ids.rearrange("(t p) f -> p t f", p=P)).then_inc(ids_in, 16)

            def source(k):
                return kern[:, k * PIECE * 2 * P:(k + 1) * PIECE * 2 * P]

            for k in range(KEPT):
                for half in range(2):
                    sp.dma_start(kept_raw[64 * half:64 * half + 64, k, :], source(k)).then_inc(kept_in, 16)

            def part_steps(part):
                for n in range(STREAMED):
                    wait_for_k_lo(sp, part, n - NR)
                    for half in range(2):
                        sp.dma_start(k_raw[64 * half:64 * half + 64, n % NR, :], source(KEPT + n)).then_inc(k_in[n % NR], 16)

            over_parts(sp, part_steps, lambda part: None)

        @block.scalar
        def _(act):
            for k in range(2):
                act.dma_start(w_ext_sb[:, k, :], w_ext[k * P:(k + 1) * P, :]).then_inc(fold_in, 16)
                act.dma_start(w1_sb[:, k, :], w1[k * P:(k + 1) * P, :]).then_inc(fold_in, 16)
            act.dma_start(w_ext_sb[0:DENSE, 2, :], w_ext[D1:D1 + DENSE, :]).then_inc(fold_in, 16)
            act.dma_start(w1_sb[0:DENSE, 2, :], w1[D1:D1 + DENSE, :]).then_inc(fold_in, 16)
            act.dma_start(b0_sb[:], b0).then_inc(fold_in, 16)
            act.dma_start(b1_sb[:], b1).then_inc(weights_in, 16)
            act.dma_start(b2_sb[:], b2).then_inc(weights_in, 16)
            act.dma_start(w2_sb[:], w2.rearrange("(k p) n -> p k n", p=P)).then_inc(weights_in, 16)
            act.dma_start(w3_sb[:], w3).then_inc(weights_in, 16)
            act.wait_ge(fold_ps, 1)
            nc.scalar.copy(w_fold[:], t_ps[:, 0:2].rearrange("p a b n -> p (a b) n")).then_inc(w_folded, 1)
            act.wait_ge(weights_in, 64)
            act.wait_ge(b_folded, 1)

            act.wait_ge(kept_in, KEPT * 32)
            for k in range(KEPT):
                nc.scalar.copy(k_hi[:, k, :], kept_raw[:, k, :]).then_inc(kept_hi_ready, 1)

            def split_piece(part, n):
                wait(act, k_in[n % NR], part, STREAMED // NR * 32, (n // NR + 1) * 32)
                wait_for_k_buffer(act, part, n)
                nc.scalar.copy(k_hi[:, KEPT + n % NK, :], k_raw[:, n % NR, :]).then_inc(k_hi_ready, 1)

            def copy_block(part, c):
                wait(act, transposed, part, BLOCKS, c + 1)
                wait(act, prod_ready, part, NU, LAST_USE[c] + 1 - NU)
                nc.scalar.copy(emb_t[:, c, :], t_buffer(TRANSPOSE, c)).then_inc(emb_ready, 1)

            def split_block(part, c):
                wait(act, emb_ready, part, BLOCKS, c + 1)
                wait(act, t_ready, part, NU, LAST_Q_USE[c - NM] + 1 if c >= NM else LAST_Q_USE[c - NM] + 1 - NU)
                for jj in range(2):
                    rows = slice(EMB * jj, EMB * jj + EMB)
                    nc.scalar.copy(q_split[rows, c % NM, jj, :], emb_t[rows, c, :]).then_inc(q_hi_ready, 1)

            def copy_pij(part, kt):
                wait(act, summed, part, NS, (kt + 1) * SUMS_PER_KT)
                wait(act, h1_ps, part, M1, 0)
                nc.scalar.copy(pij[:, kt, :], acc_ps[:, kt % NA, :]).then_inc(pij_ready, 1)
                wait(act, pij_ready, part, KT, kt + 1)
                for n, (at_kt, row) in enumerate(DENSE_ROWS):
                    if at_kt == kt:
                        act.dma_start(pij[row:row + 1, kt, :], dense_t[n:n + 1, bass.ds(part * PB, PB)]).then_inc(dense_in[kt], 16)

            def relu1(part, m):
                wait(act, h1_ps, part - 1, M1, m + 1)
                nc.scalar.activation(h1_sb[:, m, :], t_buffer(LAYER1, m), ACT.Relu, bias=b1_fold[:, m:m + 1]).then_inc(h1_ready, 1)

            def relu2(part, m):
                wait(act, h2_ps, part - 1, M2, m + 1)
                nc.scalar.activation(h2_sb[:, m, :], t_buffer(LAYER2, m), ACT.Relu, bias=b2_sb[:, m:m + 1]).then_inc(h2_ready, 1)

            def copy_y(part, _):
                wait(act, y_ps, part - 1, 1, 1)
                if not (isinstance(part, int) and part < 2):
                    wait(act, out_done, part - 1, 16, 0)
                nc.scalar.copy(y_sb[:], t_buffer(LAYER3, 0)[0:1, :]).then_inc(y_ready, 1)
                wait(act, y_ready, part, 1, 0)
                act.dma_start(out[:, bass.ds(part * PB - PB, PB)], y_sb[:]).then_inc(out_done, 16)

            mlp = [(u + 1, 0, relu1, m) for m, u in enumerate(LAYER1_AT)]
            mlp += [(u + 1, 0, relu2, m) for m, u in enumerate(LAYER2_AT)]
            mlp += [(LAYER3_AT[0] + 1, 0, copy_y, 0)]
            steps = [(PIECE * (KEPT + n - 3) + 1, 0, split_piece, n) for n in range(STREAMED)]
            steps += [(TRANSPOSE_AT[c], 2 * c + 1, copy_block, c) for c in range(BLOCKS)]
            steps += [(min(TRANSPOSE_AT[c] + 1, FIRST_USE[c]), 2 * c + 2, split_block, c) for c in range(BLOCKS)]
            steps += [(KT_TILES // 2 * (kt + 1) + SUM_UNITS + 1, 0, copy_pij, kt) for kt in range(KT)]

            def part_steps(part):
                first = isinstance(part, int)
                for _, _, step, n in sorted(steps + mlp * (not first), key=lambda s: s[:2]):
                    step(part, n)

            def last_mlp(part):
                for _, _, step, n in mlp:
                    step(part + 1, n)

            over_parts(act, part_steps, last_mlp)
            act.wait_ge(out_done, 16 * PARTS)

        @block.vector
        def _(dve):
            nc.vector.memset(selector[:], 0.0).then_inc(selector_ready, 1)
            dve.wait_ge(selector_ready, 1)
            nc.vector.memset(selector[0:EMB, 30:31], 1.0).then_inc(selector_ready, 1)
            nc.vector.memset(selector[EMB:P, 31:32], 1.0).then_inc(selector_ready, 1)
            dve.wait_ge(fold_ps, 1)
            dve.wait_ge(weights_in, 64)
            nc.vector.tensor_tensor(b1_fold[:], t_ps[:, 2, 0, 0:M1], b1_sb[:], ALU.add).then_inc(b_folded, 1)
            dve.wait_ge(w_folded, 1)

            def split_block(part, c):
                for jj in range(2):
                    wait(dve, q_hi_ready, part, FIELDS, 2 * c + jj + 1)
                    rows, others = (slice(EMB * x, EMB * x + EMB) for x in (jj, 1 - jj))
                    nc.vector.tensor_tensor(q_split[others, c % NM, jj, :], emb_t[rows, c, :],
                                            q_split[rows, c % NM, jj, :].bitcast(F32), ALU.subtract).then_inc(q_lo_ready, 1)

            def multiply(part, u):
                (c, m, _), (c2, m2, _) = UNITS[u]
                wait(dve, t_ready, part, NU, u + 1)
                wait(dve, emb_ready, part, BLOCKS, m2 + 1)
                wait(dve, summed, part, NS, (u - NP) // SUM_UNITS + 1)
                p = emb_t[:, m:m + 1, :].broadcast_to([P, 2, PB]) if m == m2 else emb_t[:, m:m + 2, :]
                nc.vector.tensor_tensor(prod[:, u % NP], t_buffer(PRODUCT, u), p, ALU.mult).then_inc(prod_ready, 1)

            for k in range(KEPT):
                dve.wait_ge(kept_hi_ready, k + 1)
                nc.vector.tensor_tensor(k_lo[:, k, :], kept_raw[:, k, :], k_hi[:, k, :].bitcast(F32),
                                        ALU.subtract).then_inc(kept_lo_ready, 1)

            def split_piece(part, n):
                split_piece_lo(dve, part, n)

            steps = [(min(TRANSPOSE_AT[c] + 2, FIRST_USE[c]), 1, split_block, c) for c in range(BLOCKS)]
            steps += [(u, 2, multiply, u) for u in range(NU)]

            def part_steps(part):
                pieces = [(PIECE * (KEPT + n - 3) + 2, 0, split_piece, n) for n in range(vector_pieces(part))]
                for _, _, step, n in sorted(pieces + steps, key=lambda s: s[:2]):
                    step(part, n)

            over_parts(dve, part_steps, lambda part: None)

        @block.tensor
        def _(pe):
            pe.wait_ge(fold_in, 7 * 16)
            for kt in range(KT):
                for k in range(3):
                    rows = P if k < 2 else DENSE
                    nc.tensor.matmul(t_ps[:, kt // 2, kt % 2, :], w_ext_sb[0:rows, k, kt * P:(kt + 1) * P], w1_sb[0:rows, k, :],
                                     start=k == 0, stop=k == 2)
            for m in range(M1):
                for k in range(2):
                    last = nc.tensor.matmul(t_ps[:, 2, 0, m:m + 1], w1_sb[:, k, m * P:(m + 1) * P], b0_sb[:, k:k + 1],
                                            start=k == 0, stop=k == 1)
            last.then_inc(fold_ps, 1)
            pe.wait_ge(w_folded, 1)
            pe.wait_ge(b_folded, 1)
            pe.wait_ge(ident_ready, 1)
            pe.wait_ge(selector_ready, 3)

            def wait_for_buffer(part, what, n):
                before, part_before = before_in_buffer((what, n), part)
                if before is None:
                    return
                what, n = before
                if what == PRODUCT:
                    wait(pe, prod_ready, part, NU, n + 1 - NU * part_before)
                elif what == TRANSPOSE:
                    wait(pe, emb_ready, part, BLOCKS, n + 1)
                else:
                    semaphore, steps = {LAYER1: (h1_ready, M1), LAYER2: (h2_ready, M2), LAYER3: (y_ready, 1)}[what]
                    wait(pe, semaphore, part - 1, steps, n + 1)

            def transpose_block(part, c):
                wait(pe, gather_in[c % NE], part, BLOCKS // NE * 2 * BT * 16, (c // NE + 1) * 2 * BT * 16)
                wait_for_buffer(part, TRANSPOSE, c)
                for bt in range(BT):
                    last = nc.tensor.transpose(t_buffer(TRANSPOSE, c)[:, bt * P:(bt + 1) * P], gathered[:, c % NE, bt, :], ident[:])
                last.then_inc(transposed, 1)

            def interact(part, u):
                k = u // PIECE
                if u % PIECE == 0 and k >= KEPT:
                    wait_for_k_lo(pe, part, k - KEPT)
                if u == 0 and isinstance(part, int):
                    pe.wait_ge(kept_lo_ready, KEPT)
                at = k if k < KEPT else KEPT + (k - KEPT) % NK
                newest = max(c for c, _, _ in UNITS[u])
                if u == FIRST_USE[newest]:
                    wait(pe, q_lo_ready, part, FIELDS, 2 * newest + 2)
                wait_for_buffer(part, PRODUCT, u)
                for n, (c, m, jj) in enumerate(UNITS[u]):
                    cols = slice((u % PIECE * 2 + n) * P, (u % PIECE * 2 + n + 1) * P)
                    for half, kk in enumerate((k_hi, k_lo)):
                        last = nc.tensor.matmul(t_buffer(PRODUCT, u)[:, n, :], kk[:, at, cols], q_split[:, c % NM, jj, :],
                                                start=half == 0, stop=half == 1)
                last.then_inc(t_ready, 1)

            def sum_products(part, s):
                kt = s // SUMS_PER_KT
                if s % SUMS_PER_KT == 0:
                    wait(pe, pij_ready, part, KT, kt - NA + 1)
                wait(pe, prod_ready, part, NU, SUM_UNITS * (s + 1))
                for t in range(2 * SUM_UNITS * s, 2 * SUM_UNITS * (s + 1)):
                    col, slot = t % COLS, t // COLS % SLOTS
                    last = nc.tensor.matmul(acc_ps[32 * col:32 * col + 32, kt % NA, :], selector[:, 30 - 2 * slot:62 - 2 * slot],
                                            prod[:, t // 2 % NP, t % 2, :], start=slot == 0, stop=slot == SLOTS - 1)
                last.then_inc(summed, 1)

            def layer1(part, m):
                wait_for_buffer(part, LAYER1, m)
                for kt in range(KT):
                    if m == 0:
                        wait(pe, pij_ready, part, KT, kt + 1 - KT)
                        wait(pe, dense_in[kt], part, 16 * sum(at == kt for at, _ in DENSE_ROWS), 0)
                    last = nc.tensor.matmul(t_buffer(LAYER1, m), w_fold[:, kt, m * P:(m + 1) * P], pij[:, kt, :],
                                            start=kt == 0, stop=kt == KT - 1)
                last.then_inc(h1_ps, 1)

            def layer2(part, m):
                wait(pe, h1_ready, part, M1, 0)
                wait_for_buffer(part, LAYER2, m)
                for k in range(M1):
                    last = nc.tensor.matmul(t_buffer(LAYER2, m), w2_sb[:, k, m * P:(m + 1) * P], h1_sb[:, k, :],
                                            start=k == 0, stop=k == M1 - 1)
                last.then_inc(h2_ps, 1)

            def layer3(part, _):
                wait(pe, h2_ready, part, M2, 0)
                wait_for_buffer(part, LAYER3, 0)
                for k in range(M2):
                    last = nc.tensor.matmul(t_buffer(LAYER3, 0)[0:1, :], w3_sb[:, k:k + 1], h2_sb[:, k, :],
                                            start=k == 0, stop=k == M2 - 1)
                last.then_inc(y_ps, 1)

            run = {TRANSPOSE: transpose_block, LAYER1: layer1, LAYER2: layer2, LAYER3: layer3,
                   PRODUCT: interact, SUMS: sum_products}

            def part_steps(part):
                for _, what, n in ORDER:
                    if what not in MLP or not isinstance(part, int):
                        run[what](part, n)

            def last_mlp(part):
                wait(pe, prod_ready, part, NU, NU)
                for _, what, n in ORDER:
                    if what in MLP:
                        run[what](part + 1, n)

            over_parts(pe, part_steps, last_mlp)


def tile_layout(L0_rec_kernel, L0_rec_W):
    pair = {}
    for i in range(FIELDS):
        for j in range(i + 1, FIELDS):
            pair[i, j] = len(pair)
    kern = np.zeros((EMB, NT, 2, EMB), L0_rec_kernel.dtype)
    w_ext = np.zeros((D1 + DENSE, KT, P), L0_rec_W.dtype)
    for t, (c, m, jj) in enumerate(TILES):
        for parity in range(2):
            i, j = 2 * m + parity, 2 * c + jj
            if i < j:
                kern[:, t, parity, :] = L0_rec_kernel[:, pair[i, j], :]
                kt, row = pij_row(t, parity)
                w_ext[0:D1, kt, row] = L0_rec_W[:, pair[i, j]]
    for n, (kt, row) in enumerate(DENSE_ROWS):
        w_ext[D1 + n, kt, row] = 1
    return kern.reshape(EMB, NT * P), w_ext.reshape(D1 + DENSE, KT * P)


def kernel(**inputs):
    import concourse.bacc as bacc
    from concourse.bass_utils import run_bass_kernel_spmd

    nc = bacc.Bacc("TRN2", target_bir_lowering=False, num_devices=1)
    arrays = {}

    def given(name, a):
        a = np.ascontiguousarray(a)
        arrays[name] = a
        return nc.dram_tensor(name, a.shape, mybir.dt.from_np(a.dtype), kind="ExternalInput").ap()

    def by_partition(v):
        return np.asarray(v).reshape(-1, P).T

    kern, w_ext = tile_layout(np.asarray(inputs["L0_rec_kernel"]), np.asarray(inputs["L0_rec_W"]))
    tables = [given(f"tbl_{f}", np.asarray(inputs[f"tbl_{f}"])) for f in range(FIELDS)]
    out = nc.dram_tensor("y", (1, BATCH), F32, kind="ExternalOutput").ap()
    dlrm_program(
        nc, given("ids", np.asarray(inputs["ids"])), tables, given("kern", kern), given("w_ext", w_ext),
        given("dense_t", np.asarray(inputs["dense_ctx"]).T), given("w1", np.asarray(inputs["W_top1"])),
        given("b1", by_partition(inputs["b_top1"])), given("w2", np.asarray(inputs["W_top2"])),
        given("b2", by_partition(inputs["b_top2"])), given("w3", by_partition(inputs["W_top3"])),
        given("b0", by_partition(inputs["L0_rec_b"])), out)
    r = run_bass_kernel_spmd(nc, [arrays], core_ids=[0])
    return r.results[0]["y"].reshape(BATCH, 1)
```

```python
from contextlib import ExitStack

import numpy as np

import concourse.bass as bass
from concourse import mybir

F32, F32R, I32 = mybir.dt.float32, mybir.dt.float32r, mybir.dt.int32
ALU = mybir.AluOpType
ACT = mybir.ActivationFunctionType

BATCH, FIELDS, EMB, DENSE = 2048, 32, 64, 16
D1, H1, H2 = 256, 512, 256
P = 128

PB = 512
PARTS = BATCH // PB
BT = PB // P
BLOCKS = FIELDS // 2
M1, M2 = H1 // P, H2 // P

UNITS = []
for _c in range(BLOCKS):
    UNITS += [((_c, m, 0), (_c, m, 1)) for m in range(_c)]
    if _c % 2 == 0:
        UNITS.append(((_c, _c, 1), (_c + 1, _c + 1, 1)))
TILES = [tile for unit in UNITS for tile in unit]
NU, NT = len(UNITS), len(TILES)
FIRST_USE = [min(u for u in range(NU) if any(tile[0] == c for tile in UNITS[u])) for c in range(BLOCKS)]
LAST_Q_USE = [max(u for u in range(NU) if any(tile[0] == c for tile in UNITS[u])) for c in range(BLOCKS)]
LAST_USE = [max(u for u in range(NU) if any(tile[1] == c for tile in UNITS[u])) for c in range(BLOCKS)]

COLS = 4
SLOTS = 16
KT_TILES = COLS * SLOTS
KT = NT // KT_TILES
SUM_UNITS = 4
SUM_LAG = 3
NS = NU // SUM_UNITS
SUMS_PER_KT = NS // KT
PIECE = 4
PIECES = NU // PIECE
KEPT = 4
STREAMED = PIECES - KEPT
VECTOR_PIECES_FIRST, VECTOR_PIECES = 20, 10

NE, NP, NTB, NM, NR, NK = 8, 8, 3, 4, 2, 4


def pij_row(t, parity):
    return t // KT_TILES, 32 * (t % COLS) + 2 * (t // COLS % SLOTS) + parity


DENSE_ROWS = [pij_row(TILES.index((c, c, 1)), 1) for c in range(BLOCKS)]

TRANSPOSE_AT_FIRST = [-1, 0, 2, 4] + [FIRST_USE[c] - min(2 * c - 6, 8) for c in range(4, BLOCKS)]
TRANSPOSE_AT = [3 * c - 12 if c < 4 else FIRST_USE[c] - 8 for c in range(BLOCKS)]
SPLIT_AT = [PIECE * (KEPT + n - 3) for n in range(STREAMED)]
SPLIT_AT_FIRST = [3 * n if n < NK else SPLIT_AT[n] for n in range(STREAMED)]
GATHER_LATE = 14
TAIL = 12

TRANSPOSE, FOLD, LAYER1, LAYER2, LAYER3, PRODUCT, SUMS = range(7)
FOLD_AT = (-1, 0, 2, 4, 8)
LAYER1_AT, LAYER2_AT, LAYER3_AT = [NU + u for u in (8, 14, 20, 26)], [NU + u for u in (32, 38)], NU + 44
SUMS_AT = [SUM_UNITS * (s + 1) + SUM_LAG - 1 for s in range(NS)]
PIJ_AT = [SUMS_AT[(kt + 1) * SUMS_PER_KT - 1] + 2 for kt in range(KT)]


def iteration_steps(steps, first=False, last=False):
    placed = [(at, rank, step, n, 0) for at, rank, step, n in steps if at < NU - TAIL and not last]
    placed += [(at - NU, rank, step, n, 1) for at, rank, step, n in steps if at >= NU - TAIL and not first]
    return [x[2:] for x in sorted(placed, key=lambda x: x[:2])]


def tensor_steps(first):
    steps = [(at, TRANSPOSE, TRANSPOSE, c) for c, at in enumerate(TRANSPOSE_AT_FIRST if first else TRANSPOSE_AT)]
    steps += [(at, LAYER1, LAYER1, m) for m, at in enumerate(LAYER1_AT)]
    steps += [(at, LAYER2, LAYER2, m) for m, at in enumerate(LAYER2_AT)]
    steps += [(LAYER3_AT, LAYER3, LAYER3, 0)]
    steps += [(at, FOLD, FOLD, n) for n, at in enumerate(FOLD_AT) if first]
    steps += [(u, PRODUCT, PRODUCT, u) for u in range(NU)]
    return steps + [(at, SUMS, SUMS, s) for s, at in enumerate(SUMS_AT)]


def before_in_side(user, behind, first, last):
    def users(first, last):
        return [(what, n, d) for what, n, d in iteration_steps(tensor_steps(first), first, last) if what < PRODUCT]
    own = users(first, last)
    at = own.index((*user, behind))
    if at:
        what, n, d = own[at - 1]
        return (what, n), d - behind
    if first or last:
        return None
    what, n, d = own[-1]
    return (what, n), d + 1 - behind


def dlrm_program(nc, ids, tables, kern, w_ext, dense_t, w1, b1, w2, b2, w3, b0, out):
    ctx = ExitStack()
    with ctx:
        def sb(name, shape, dt=F32):
            return ctx.enter_context(nc.sbuf_tensor(name, shape, dt))

        def sem(name):
            return ctx.enter_context(nc.semaphore(name))

        ids_sb = sb("ids_sb", [P, PARTS * BT * FIELDS], I32)
        ident = sb("ident", [P, P])
        selector = sb("selector", [P, 62])
        gathered = sb("gathered", [P, NE, BT, 2 * EMB])
        emb_t = sb("emb_t", [P, BLOCKS, PB])
        q_split = sb("q_split", [P, NM, 2, PB], F32R)
        k_raw = sb("k_raw", [P, NR, PIECE * 2 * P])
        k_hi = sb("k_hi", [P, KEPT + NK, PIECE * 2 * P], F32R)
        k_lo = sb("k_lo", [P, KEPT + NK, PIECE * 2 * P], F32R)
        prod = sb("prod", [P, NP, 2, PB])
        pij = sb("pij", [P, KT, PB])
        h1_sb = sb("h1_sb", [P, M1, PB])
        h2_sb = sb("h2_sb", [P, M2, PB])
        y_sb = sb("y_sb", [P, PB // COLS])
        w_fold = sb("w_fold", [P, KT, H1])
        w2_sb = sb("w2_sb", [P, M1, H2])
        w3_raw = sb("w3_raw", [P, M2])
        w3_sb = sb("w3_sb", [P, M2, P // COLS])
        b0_sb = sb("b0_sb", [P, D1 // P])
        b1_sb = sb("b1_sb", [P, M1])
        b1_fold = sb("b1_fold", [P, M1])
        b2_sb = sb("b2_sb", [P, M2])
        w_ext_sb = h1_sb[:, 0:3, :]
        w1_sb = [h1_sb[:, 3, :], h2_sb[:, 0, :], h2_sb[:, 1, :]]
        kept_raw = prod[:, NP - KEPT:NP].rearrange("p k a n -> p k (a n)")

        t_ps = ctx.enter_context(nc.psum_tensor("t_ps", [P, NTB, 2, PB], F32))
        side_ps = ctx.enter_context(nc.psum_tensor("side_ps", [P, PB], F32))
        acc_ps = ctx.enter_context(nc.psum_tensor("acc_ps", [P, PB], F32))

        def mlp_bank(part, what, n):
            if not isinstance(part, int) or what == LAYER3:
                return side_ps[:]
            at = n if what == LAYER1 else M1 + n
            return t_ps[:, at // 2, at % 2, :]

        ids_in = sem("ids_in")
        zeroed = sem("zeroed")
        ident_ready = sem("ident_ready")
        selector_ready = sem("selector_ready")
        fold_in = sem("fold_in")
        w3_zeroed = sem("w3_zeroed")
        w3_ready = sem("w3_ready")
        weights_in = sem("weights_in")
        fold_ps = sem("fold_ps")
        w_folded = sem("w_folded")
        b_folded = sem("b_folded")
        gather_in = [sem(f"gather_in{n}") for n in range(NE)]
        transposed = sem("transposed")
        emb_ready = sem("emb_ready")
        q_hi_ready = sem("q_hi_ready")
        q_lo_ready = sem("q_lo_ready")
        kept_in = sem("kept_in")
        kept_hi_ready = sem("kept_hi_ready")
        kept_lo_ready = sem("kept_lo_ready")
        k_in = [sem(f"k_in{n}") for n in range(NR)]
        k_hi_ready = sem("k_hi_ready")
        k_lo_vector = sem("k_lo_vector")
        k_lo_pool = sem("k_lo_pool")
        t_ready = sem("t_ready")
        prod_ready = sem("prod_ready")
        summed = sem("summed")
        pij_ready = sem("pij_ready")
        dense_in = [sem(f"dense_in{kt}") for kt in range(KT)]
        h1_ps = sem("h1_ps")
        h1_ready = sem("h1_ready")
        h2_ps = sem("h2_ps")
        h2_ready = sem("h2_ready")
        y_ps = sem("y_ps")
        y_ready = sem("y_ready")
        out_done = sem("out_done")

        def wait(engine, semaphore, part, per_part, n):
            if isinstance(part, int) and part * per_part + n <= 0:
                return
            engine.wait_ge(semaphore, part * per_part + n)

        def vector_pieces(part):
            return VECTOR_PIECES_FIRST if isinstance(part, int) and part == 0 else VECTOR_PIECES

        def wait_for_k_lo(engine, part, n):
            first = isinstance(part, int) and part == 0
            by_vector = 0 <= n < vector_pieces(part)
            semaphore, in_first, in_other, at = (
                (k_lo_vector, VECTOR_PIECES_FIRST, VECTOR_PIECES, n + 1) if by_vector else
                (k_lo_pool, STREAMED - VECTOR_PIECES_FIRST, STREAMED - VECTOR_PIECES, n - vector_pieces(part) + 1 if n >= 0 else n + 1))
            wait(engine, semaphore, part, in_other, at if first else at + in_first - in_other)

        def wait_for_k_buffer(engine, part, n):
            before = n - NK + KEPT + 1 if n >= NK else n - NK + 1
            wait(engine, t_ready, part, NU, before * PIECE)

        def split_piece_lo(engine, part, n):
            wait(engine, k_hi_ready, part, STREAMED, n + 1)
            wait_for_k_buffer(engine, part, n)
            at = KEPT + n % NK
            engine.tensor_tensor(k_lo[:, at, :], k_raw[:, n % NR, :], k_hi[:, at, :].bitcast(F32),
                                 ALU.subtract).then_inc(k_lo_vector if n < vector_pieces(part) else k_lo_pool, 1)

        def over_parts(engine, steps):
            for step, n, behind in iteration_steps(steps(True), first=True):
                step(0, n)
            with engine.Fori(1, PARTS) as part:
                for step, n, behind in iteration_steps(steps(False)):
                    step(part - behind if behind else part, n)
            for step, n, behind in iteration_steps(steps(False), last=True):
                step(PARTS - 1, n)

        block = ctx.enter_context(nc.Block())

        @block.gpsimd
        def _(pool):
            nc.gpsimd.memset(ident[:], 0.0).then_inc(zeroed, 1)
            pool.wait_ge(zeroed, 1)
            nc.gpsimd.affine_select(out=ident[:], in_=ident[:], compare_op=ALU.not_equal, fill=1.0, base=0,
                                    pattern=[[-1, P]], channel_multiplier=1).then_inc(ident_ready, 1)
            pool.wait_ge(ids_in, 16)
            def gather_field(part, f):
                c, jj = divmod(f, 2)
                if jj == 0:
                    wait(pool, transposed, part, BLOCKS, c - NE + 1)
                for bt in range(BT):
                    col = (part * BT + bt) * FIELDS + f
                    nc.gpsimd.indirect_dma_start(
                        out=gathered[:, c % NE, bt, jj * EMB:(jj + 1) * EMB], out_offset=None, in_=tables[f],
                        in_offset=bass.IndirectOffsetOnAxis(ap=ids_sb[:, col:col + 1], axis=0),
                    ).then_inc(gather_in[c % NE], 16)

            def split_piece(part, n):
                split_piece_lo(pool, part, n)

            def freed_at(part, c):
                if c >= NE:
                    return (TRANSPOSE_AT if part else TRANSPOSE_AT_FIRST)[c - NE]
                return (TRANSPOSE_AT if part > 1 else TRANSPOSE_AT_FIRST)[c + NE] - NU

            steps = [(NU * part + freed_at(part, f // 2) + 2 * (f % 2) + GATHER_LATE * (part == 1 and f // 2 < NE), gather_field, part, f)
                     for part in range(PARTS) for f in range(FIELDS)]
            steps += [(NU * part + SPLIT_AT[n] + 2, split_piece, part, n)
                      for part in range(PARTS) for n in range(vector_pieces(part), STREAMED)]
            for _, step, part, n in sorted(steps, key=lambda s: s[0]):
                step(part, n)

        @block.sync
        def _(sp):
            sp.dma_start(ids_sb[:].rearrange("p (t f) -> p t f", f=FIELDS),
                         ids.rearrange("(t p) f -> p t f", p=P)).then_inc(ids_in, 16)

            def source(k):
                return kern[:, k * PIECE * 2 * P:(k + 1) * PIECE * 2 * P]

            for k in range(KEPT):
                for half in range(2):
                    sp.dma_start(kept_raw[64 * half:64 * half + 64, k, :], source(k)).then_inc(kept_in, 16)

            def part_steps(part):
                for n in range(STREAMED):
                    wait_for_k_lo(sp, part, n - NR)
                    for half in range(2):
                        sp.dma_start(k_raw[64 * half:64 * half + 64, n % NR, :], source(KEPT + n)).then_inc(k_in[n % NR], 16)

            part_steps(0)
            with sp.Fori(1, PARTS) as part:
                part_steps(part)

        @block.scalar
        def _(act):
            for k in range(2):
                act.dma_start(w_ext_sb[:, k, :], w_ext[k * P:(k + 1) * P, :]).then_inc(fold_in, 16)
                act.dma_start(w1_sb[k], w1[k * P:(k + 1) * P, :]).then_inc(fold_in, 16)
            act.dma_start(w_ext_sb[0:DENSE, 2, :], w_ext[D1:D1 + DENSE, :]).then_inc(fold_in, 16)
            act.dma_start(w1_sb[2][0:DENSE, :], w1[D1:D1 + DENSE, :]).then_inc(fold_in, 16)
            act.dma_start(b0_sb[:], b0).then_inc(fold_in, 16)
            act.dma_start(b1_sb[:], b1).then_inc(weights_in, 16)
            act.dma_start(b2_sb[:], b2).then_inc(weights_in, 16)
            act.dma_start(w2_sb[:], w2.rearrange("(k p) n -> p k n", p=P)).then_inc(weights_in, 16)
            act.dma_start(w3_raw[:], w3).then_inc(weights_in, 16)
            act.wait_ge(kept_in, KEPT * 32)
            for k in range(KEPT):
                nc.scalar.copy(k_hi[:, k, :], kept_raw[:, k, :]).then_inc(kept_hi_ready, 1)
            act.wait_ge(weights_in, 64)
            act.wait_ge(w3_zeroed, 1)
            nc.scalar.copy(w3_sb[:, :, 0], w3_raw[:]).then_inc(w3_ready, 1)

            def copy_fold(_, n):
                act.wait_ge(fold_ps, n + 1)
                if n < KT:
                    nc.scalar.copy(w_fold[:, n, :], side_ps[:]).then_inc(w_folded, 1)
                else:
                    for m in range(M1):
                        nc.scalar.activation(b1_fold[:, m:m + 1], side_ps[:, m:m + 1], ACT.Identity,
                                             bias=b1_sb[:, m:m + 1]).then_inc(b_folded, 1)

            def split_piece(part, n):
                wait(act, k_in[n % NR], part, STREAMED // NR * 32, (n // NR + 1) * 32)
                wait_for_k_buffer(act, part, n)
                nc.scalar.copy(k_hi[:, KEPT + n % NK, :], k_raw[:, n % NR, :]).then_inc(k_hi_ready, 1)

            def copy_block(part, c):
                wait(act, transposed, part, BLOCKS, c + 1)
                wait(act, prod_ready, part, NU, LAST_USE[c] + 1 - NU)
                nc.scalar.copy(emb_t[:, c, :], side_ps[:]).then_inc(emb_ready, 1)

            def split_block(part, c):
                wait(act, emb_ready, part, BLOCKS, c + 1)
                wait(act, t_ready, part, NU, LAST_Q_USE[c - NM] + 1 if c >= NM else LAST_Q_USE[c - NM] + 1 - NU)
                for jj in range(2):
                    rows = slice(EMB * jj, EMB * jj + EMB)
                    nc.scalar.copy(q_split[rows, c % NM, jj, :], emb_t[rows, c, :]).then_inc(q_hi_ready, 1)

            def copy_pij(part, kt):
                wait(act, summed, part, NS, (kt + 1) * SUMS_PER_KT)
                if kt == 0:
                    wait(act, h1_ps, part, M1, 0)
                nc.scalar.copy(pij[:, kt, :], acc_ps[:]).then_inc(pij_ready, 1)
                wait(act, pij_ready, part, KT, kt + 1)
                for n, (at_kt, row) in enumerate(DENSE_ROWS):
                    if at_kt == kt:
                        act.dma_start(pij[row:row + 1, kt, :], dense_t[n:n + 1, bass.ds(part * PB, PB)]).then_inc(dense_in[kt], 16)

            def relu1(part, m):
                wait(act, h1_ps, part, M1, m + 1)
                act.wait_ge(b_folded, M1)
                nc.scalar.activation(h1_sb[:, m, :], mlp_bank(part, LAYER1, m), ACT.Relu, bias=b1_fold[:, m:m + 1]).then_inc(h1_ready, 1)

            def relu2(part, m):
                wait(act, h2_ps, part, M2, m + 1)
                nc.scalar.activation(h2_sb[:, m, :], mlp_bank(part, LAYER2, m), ACT.Relu, bias=b2_sb[:, m:m + 1]).then_inc(h2_ready, 1)

            def copy_y(part, _):
                wait(act, y_ps, part, 1, 1)
                nc.scalar.copy(y_sb[:], side_ps[:, 0:PB // COLS]).then_inc(y_ready, 1)
                wait(act, y_ready, part, 1, 1)
                act.dma_start(out[:, bass.ds(part * PB, PB)].rearrange("o (c n) -> (o c) n", c=COLS),
                              y_sb[0:P:P // COLS, :]).then_inc(out_done, 16)

            def leave_y(part, _):
                wait(act, out_done, part, 16, 16)

            def part_steps(first):
                transpose_at = TRANSPOSE_AT_FIRST if first else TRANSPOSE_AT
                steps = [((SPLIT_AT_FIRST if first else SPLIT_AT)[n] + 1, 0, split_piece, n) for n in range(STREAMED)]
                steps += [(at, 2 * BLOCKS + 1, copy_fold, n) for n, at in enumerate(FOLD_AT) if first]
                steps += [(transpose_at[c], 2 * c + 1, copy_block, c) for c in range(BLOCKS)]
                steps += [(min(transpose_at[c] + 1, FIRST_USE[c]), 2 * c + 2, split_block, c) for c in range(BLOCKS)]
                steps += [(at, 0, copy_pij, kt) for kt, at in enumerate(PIJ_AT)]
                steps += [(at + 1, 0, relu1, m) for m, at in enumerate(LAYER1_AT)]
                steps += [(at + 1, 0, relu2, m) for m, at in enumerate(LAYER2_AT)]
                return steps + [(LAYER3_AT + 1, 0, copy_y, 0), (LAYER3_AT + 16, 0, leave_y, 0)]

            over_parts(act, part_steps)

        @block.vector
        def _(dve):
            nc.vector.memset(w3_sb[:], 0.0).then_inc(w3_zeroed, 1)
            nc.vector.memset(selector[:], 0.0).then_inc(selector_ready, 1)
            dve.wait_ge(selector_ready, 1)
            nc.vector.memset(selector[0:EMB, 30:31], 1.0).then_inc(selector_ready, 1)
            nc.vector.memset(selector[EMB:P, 31:32], 1.0).then_inc(selector_ready, 1)
            def split_block(part, c):
                for jj in range(2):
                    wait(dve, q_hi_ready, part, FIELDS, 2 * c + jj + 1)
                    rows, others = (slice(EMB * x, EMB * x + EMB) for x in (jj, 1 - jj))
                    nc.vector.tensor_tensor(q_split[others, c % NM, jj, :], emb_t[rows, c, :],
                                            q_split[rows, c % NM, jj, :].bitcast(F32), ALU.subtract).then_inc(q_lo_ready, 1)

            def multiply(part, u):
                (c, m, _), (c2, m2, _) = UNITS[u]
                wait(dve, t_ready, part, NU, u + 1)
                wait(dve, emb_ready, part, BLOCKS, m2 + 1)
                wait(dve, summed, part, NS, (u - NP) // SUM_UNITS + 1)
                p = emb_t[:, m:m + 1, :].broadcast_to([P, 2, PB]) if m == m2 else emb_t[:, m:m + 2, :]
                nc.vector.tensor_tensor(prod[:, u % NP], t_ps[:, u % NTB], p, ALU.mult).then_inc(prod_ready, 1)

            for k in range(KEPT):
                dve.wait_ge(kept_hi_ready, k + 1)
                nc.vector.tensor_tensor(k_lo[:, k, :], kept_raw[:, k, :], k_hi[:, k, :].bitcast(F32),
                                        ALU.subtract).then_inc(kept_lo_ready, 1)

            def split_piece(part, n):
                split_piece_lo(dve, part, n)

            def part_steps(first):
                transpose_at, pieces = (TRANSPOSE_AT_FIRST, VECTOR_PIECES_FIRST) if first else (TRANSPOSE_AT, VECTOR_PIECES)
                steps = [((SPLIT_AT_FIRST if first else SPLIT_AT)[n] + 2, 0, split_piece, n) for n in range(pieces)]
                steps += [(min(transpose_at[c] + 3, FIRST_USE[c]), 1, split_block, c) for c in range(BLOCKS)]
                return steps + [(u, 2, multiply, u) for u in range(NU)]

            over_parts(dve, part_steps)

        @block.tensor
        def _(pe):
            pe.wait_ge(ident_ready, 1)
            pe.wait_ge(selector_ready, 3)

            def wait_for_side(part, behind, kind, what, n):
                before = before_in_side((what, n), behind, *kind)
                if before is None:
                    return
                (what, n), parts = before
                if what == FOLD:
                    pe.wait_ge(*((w_folded, n + 1) if n < KT else (b_folded, M1)))
                    return
                semaphore, steps = {TRANSPOSE: (emb_ready, BLOCKS), LAYER1: (h1_ready, M1), LAYER2: (h2_ready, M2),
                                    LAYER3: (y_ready, 1)}[what]
                wait(pe, semaphore, part, steps, n + 1 - steps * parts)

            def transpose_block(part, c):
                wait(pe, gather_in[c % NE], part, BLOCKS // NE * 2 * BT * 16, (c // NE + 1) * 2 * BT * 16)
                for bt in range(BT):
                    last = nc.tensor.transpose(side_ps[:, bt * P:(bt + 1) * P], gathered[:, c % NE, bt, :], ident[:])
                last.then_inc(transposed, 1)

            def fold(_, n):
                if n == 0:
                    pe.wait_ge(fold_in, 7 * 16)
                if n < KT:
                    for k in range(3):
                        rows = P if k < 2 else DENSE
                        last = nc.tensor.matmul(side_ps[:], w_ext_sb[0:rows, k, n * P:(n + 1) * P], w1_sb[k][0:rows, :],
                                                start=k == 0, stop=k == 2)
                else:
                    for m in range(M1):
                        for k in range(2):
                            last = nc.tensor.matmul(side_ps[:, m:m + 1], w1_sb[k][:, m * P:(m + 1) * P], b0_sb[:, k:k + 1],
                                                    start=k == 0, stop=k == 1)
                last.then_inc(fold_ps, 1)

            def interact(part, u):
                k = u // PIECE
                if u % PIECE == 0 and k >= KEPT:
                    wait_for_k_lo(pe, part, k - KEPT)
                if u == 0 and isinstance(part, int):
                    pe.wait_ge(kept_lo_ready, KEPT)
                at = k if k < KEPT else KEPT + (k - KEPT) % NK
                newest = max(c for c, _, _ in UNITS[u])
                if u == FIRST_USE[newest]:
                    wait(pe, q_lo_ready, part, FIELDS, 2 * newest + 2)
                wait(pe, prod_ready, part, NU, u - NTB + 1 if u >= NTB else max(range(u, NU, NTB)) + 1 - NU)
                for n, (c, m, jj) in enumerate(UNITS[u]):
                    cols = slice((u % PIECE * 2 + n) * P, (u % PIECE * 2 + n + 1) * P)
                    for half, kk in enumerate((k_hi, k_lo)):
                        last = nc.tensor.matmul(t_ps[:, u % NTB, n, :], kk[:, at, cols], q_split[:, c % NM, jj, :],
                                                start=half == 0, stop=half == 1)
                last.then_inc(t_ready, 1)

            def sum_products(part, s):
                kt = s // SUMS_PER_KT
                if s % SUMS_PER_KT == 0:
                    wait(pe, pij_ready, part, KT, kt)
                wait(pe, prod_ready, part, NU, SUM_UNITS * (s + 1))
                for t in range(2 * SUM_UNITS * s, 2 * SUM_UNITS * (s + 1)):
                    col, slot = t % COLS, t // COLS % SLOTS
                    last = nc.tensor.matmul(acc_ps[32 * col:32 * col + 32, :], selector[:, 30 - 2 * slot:62 - 2 * slot],
                                            prod[:, t // 2 % NP, t % 2, :], start=slot == 0, stop=slot == SLOTS - 1)
                last.then_inc(summed, 1)

            def layer1(part, m):
                for kt in range(KT):
                    if m == 0:
                        wait(pe, pij_ready, part, KT, kt + 1)
                        rows = sum(at == kt for at, _ in DENSE_ROWS)
                        wait(pe, dense_in[kt], part, 16 * rows, 16 * rows)
                    last = nc.tensor.matmul(mlp_bank(part, LAYER1, m), w_fold[:, kt, m * P:(m + 1) * P], pij[:, kt, :],
                                            start=kt == 0, stop=kt == KT - 1)
                last.then_inc(h1_ps, 1)

            def layer2(part, m):
                wait(pe, h1_ready, part, M1, M1)
                for k in range(M1):
                    last = nc.tensor.matmul(mlp_bank(part, LAYER2, m), w2_sb[:, k, m * P:(m + 1) * P], h1_sb[:, k, :],
                                            start=k == 0, stop=k == M1 - 1)
                last.then_inc(h2_ps, 1)

            def layer3(part, _):
                wait(pe, h2_ready, part, M2, M2)
                pe.wait_ge(w3_ready, 1)
                for k in range(M2):
                    for col in range(COLS):
                        last = nc.tensor.matmul(side_ps[P // COLS * col:P // COLS * (col + 1), 0:PB // COLS], w3_sb[:, k, :],
                                                h2_sb[:, k, PB // COLS * col:PB // COLS * (col + 1)],
                                                start=k == 0, stop=k == M2 - 1)
                last.then_inc(y_ps, 1)

            run = {TRANSPOSE: transpose_block, FOLD: fold, LAYER1: layer1, LAYER2: layer2, LAYER3: layer3,
                   PRODUCT: interact, SUMS: sum_products}

            def iteration(part, first, last):
                for what, n, behind in iteration_steps(tensor_steps(first), first, last):
                    own = part - behind if behind else part
                    if what < PRODUCT and not last:
                        wait_for_side(own, behind, (first, last), what, n)
                    run[what](own, n)

            iteration(0, True, False)
            with pe.Fori(1, PARTS) as part:
                iteration(part, False, False)
            iteration(PARTS, False, True)

def tile_layout(L0_rec_kernel, L0_rec_W):
    pair = {}
    for i in range(FIELDS):
        for j in range(i + 1, FIELDS):
            pair[i, j] = len(pair)
    kern = np.zeros((EMB, NT, 2, EMB), L0_rec_kernel.dtype)
    w_ext = np.zeros((D1 + DENSE, KT, P), L0_rec_W.dtype)
    for t, (c, m, jj) in enumerate(TILES):
        for parity in range(2):
            i, j = 2 * m + parity, 2 * c + jj
            if i < j:
                kern[:, t, parity, :] = L0_rec_kernel[:, pair[i, j], :]
                kt, row = pij_row(t, parity)
                w_ext[0:D1, kt, row] = L0_rec_W[:, pair[i, j]]
    for n, (kt, row) in enumerate(DENSE_ROWS):
        w_ext[D1 + n, kt, row] = 1
    return kern.reshape(EMB, NT * P), w_ext.reshape(D1 + DENSE, KT * P)


def kernel(**inputs):
    import concourse.bacc as bacc
    from concourse.bass_utils import run_bass_kernel_spmd

    nc = bacc.Bacc("TRN2", target_bir_lowering=False, num_devices=1)
    arrays = {}

    def given(name, a):
        a = np.ascontiguousarray(a)
        arrays[name] = a
        return nc.dram_tensor(name, a.shape, mybir.dt.from_np(a.dtype), kind="ExternalInput").ap()

    def by_partition(v):
        return np.asarray(v).reshape(-1, P).T

    kern, w_ext = tile_layout(np.asarray(inputs["L0_rec_kernel"]), np.asarray(inputs["L0_rec_W"]))
    tables = [given(f"tbl_{f}", np.asarray(inputs[f"tbl_{f}"])) for f in range(FIELDS)]
    out = nc.dram_tensor("y", (1, BATCH), F32, kind="ExternalOutput").ap()
    dlrm_program(
        nc, given("ids", np.asarray(inputs["ids"])), tables, given("kern", kern), given("w_ext", w_ext),
        given("dense_t", np.asarray(inputs["dense_ctx"]).T), given("w1", np.asarray(inputs["W_top1"])),
        given("b1", by_partition(inputs["b_top1"])), given("w2", np.asarray(inputs["W_top2"])),
        given("b2", by_partition(inputs["b_top2"])), given("w3", by_partition(inputs["W_top3"])),
        given("b0", by_partition(inputs["L0_rec_b"])), out)
    r = run_bass_kernel_spmd(nc, [arrays], core_ids=[0])
    return r.results[0]["y"].reshape(BATCH, 1)
```
